# Optimizing a Trainium2 kernel written in Bass

```python
import numpy as np
import jax
import jax.numpy as jnp

def _softmax(x, axis=-1):
    return jax.nn.softmax(x, axis=axis)

def _gelu(x):
    return jax.nn.gelu(x, approximate=True)

def _silu(x):
    return jax.nn.silu(x)

def _sigmoid(x):
    return jax.nn.sigmoid(x)

def _layernorm(x, axis=-1, eps=1e-05):
    m = jnp.mean(x, axis=axis, keepdims=True)
    v = jnp.var(x, axis=axis, keepdims=True)
    return (x - m) / jnp.sqrt(v + eps)

def _scatter_add(tgt, idx, src, axis=0):
    return tgt.at[idx].add(src)

def _segment_sum(src, seg, n):
    return jax.ops.segment_sum(src, seg, n)
kernel_name = 'mk_dlrm_tower_d1_rec_r8_eaf02a'

def setup_inputs(seed: int=0):
    np.random.seed(seed)
    _w = jnp.asarray

    def _rec_inputs():
        import jax
        import jax.numpy as jnp
        _tk = jax.random.key(seed)
        ids = jnp.stack([jax.random.randint(jax.random.fold_in(_tk, 200 + f), (512,), 0, v, jnp.int32) for f, v in enumerate([125000, 1250, 1250, 12500, 1250, 12500, 12500, 1000, 1250, 1250, 12500, 1250, 12500, 12500, 1000, 12500, 1250, 1000, 1250, 1000, 1000, 12500, 1000, 1000, 1000, 1000])], axis=1)
        tbl_0 = 0.05 * jax.random.normal(jax.random.fold_in(_tk, 500 + 0), (125000, 128), jnp.float32)
        tbl_1 = 0.05 * jax.random.normal(jax.random.fold_in(_tk, 500 + 1), (1250, 128), jnp.float32)
        tbl_2 = 0.05 * jax.random.normal(jax.random.fold_in(_tk, 500 + 2), (1250, 128), jnp.float32)
        tbl_3 = 0.05 * jax.random.normal(jax.random.fold_in(_tk, 500 + 3), (12500, 128), jnp.float32)
        tbl_4 = 0.05 * jax.random.normal(jax.random.fold_in(_tk, 500 + 4), (1250, 128), jnp.float32)
        tbl_5 = 0.05 * jax.random.normal(jax.random.fold_in(_tk, 500 + 5), (12500, 128), jnp.float32)
        tbl_6 = 0.05 * jax.random.normal(jax.random.fold_in(_tk, 500 + 6), (12500, 128), jnp.float32)
        tbl_7 = 0.05 * jax.random.normal(jax.random.fold_in(_tk, 500 + 7), (1000, 128), jnp.float32)
        tbl_8 = 0.05 * jax.random.normal(jax.random.fold_in(_tk, 500 + 8), (1250, 128), jnp.float32)
        tbl_9 = 0.05 * jax.random.normal(jax.random.fold_in(_tk, 500 + 9), (1250, 128), jnp.float32)
        tbl_10 = 0.05 * jax.random.normal(jax.random.fold_in(_tk, 500 + 10), (12500, 128), jnp.float32)
        tbl_11 = 0.05 * jax.random.normal(jax.random.fold_in(_tk, 500 + 11), (1250, 128), jnp.float32)
        tbl_12 = 0.05 * jax.random.normal(jax.random.fold_in(_tk, 500 + 12), (12500, 128), jnp.float32)
        tbl_13 = 0.05 * jax.random.normal(jax.random.fold_in(_tk, 500 + 13), (12500, 128), jnp.float32)
        tbl_14 = 0.05 * jax.random.normal(jax.random.fold_in(_tk, 500 + 14), (1000, 128), jnp.float32)
        tbl_15 = 0.05 * jax.random.normal(jax.random.fold_in(_tk, 500 + 15), (12500, 128), jnp.float32)
        tbl_16 = 0.05 * jax.random.normal(jax.random.fold_in(_tk, 500 + 16), (1250, 128), jnp.float32)
        tbl_17 = 0.05 * jax.random.normal(jax.random.fold_in(_tk, 500 + 17), (1000, 128), jnp.float32)
        tbl_18 = 0.05 * jax.random.normal(jax.random.fold_in(_tk, 500 + 18), (1250, 128), jnp.float32)
        tbl_19 = 0.05 * jax.random.normal(jax.random.fold_in(_tk, 500 + 19), (1000, 128), jnp.float32)
        tbl_20 = 0.05 * jax.random.normal(jax.random.fold_in(_tk, 500 + 20), (1000, 128), jnp.float32)
        tbl_21 = 0.05 * jax.random.normal(jax.random.fold_in(_tk, 500 + 21), (12500, 128), jnp.float32)
        tbl_22 = 0.05 * jax.random.normal(jax.random.fold_in(_tk, 500 + 22), (1000, 128), jnp.float32)
        tbl_23 = 0.05 * jax.random.normal(jax.random.fold_in(_tk, 500 + 23), (1000, 128), jnp.float32)
        tbl_24 = 0.05 * jax.random.normal(jax.random.fold_in(_tk, 500 + 24), (1000, 128), jnp.float32)
        tbl_25 = 0.05 * jax.random.normal(jax.random.fold_in(_tk, 500 + 25), (1000, 128), jnp.float32)
        _rk = jax.random.fold_in(_tk, 7)
        r_dense_features = -0.000520686 + 1.00062 * jax.random.normal(jax.random.fold_in(_rk, 101), (512, 128), jnp.float32)
        W_top1 = 0.0405887 * jax.random.normal(jax.random.fold_in(_tk, 801), (607, 512), jnp.float32)
        W_top2 = 0.0441942 * jax.random.normal(jax.random.fold_in(_tk, 802), (512, 256), jnp.float32)
        W_top3 = 0.0625 * jax.random.normal(jax.random.fold_in(_tk, 803), (256, 1), jnp.float32)
        b_top1 = jnp.zeros((512,), jnp.float32)
        b_top2 = jnp.zeros((256,), jnp.float32)
        return (r_dense_features, ids, tbl_0, tbl_1, tbl_2, tbl_3, tbl_4, tbl_5, tbl_6, tbl_7, tbl_8, tbl_9, tbl_10, tbl_11, tbl_12, tbl_13, tbl_14, tbl_15, tbl_16, tbl_17, tbl_18, tbl_19, tbl_20, tbl_21, tbl_22, tbl_23, tbl_24, tbl_25, W_top1, b_top1, W_top2, b_top2, W_top3)
    r_dense_features, ids, tbl_0, tbl_1, tbl_2, tbl_3, tbl_4, tbl_5, tbl_6, tbl_7, tbl_8, tbl_9, tbl_10, tbl_11, tbl_12, tbl_13, tbl_14, tbl_15, tbl_16, tbl_17, tbl_18, tbl_19, tbl_20, tbl_21, tbl_22, tbl_23, tbl_24, tbl_25, W_top1, b_top1, W_top2, b_top2, W_top3 = _rec_inputs()

    def _L0_rec_setup():
        import jax, jax.numpy as jnp
        import numpy as np
        NUM_SPARSE = 26
        EMBED_DIM = 128
        BATCH = 2048
        key = jax.random.key(seed)
        k1, k2 = jax.random.split(key)
        dense_features = jax.random.normal(k1, (BATCH, EMBED_DIM), dtype=jnp.float32)
        sparse_features = jax.random.normal(k2, (BATCH, NUM_SPARSE, EMBED_DIM), dtype=jnp.float32)
        return {'dense_features': dense_features, 'sparse_features': sparse_features}
    _L0_rec_all = _L0_rec_setup()
    _L0_rec_in = {k: v for k, v in _L0_rec_all.items() if k in ()}
    del _L0_rec_all
    return {'r_dense_features': r_dense_features, 'ids': ids, 'tbl_0': tbl_0, 'tbl_1': tbl_1, 'tbl_2': tbl_2, 'tbl_3': tbl_3, 'tbl_4': tbl_4, 'tbl_5': tbl_5, 'tbl_6': tbl_6, 'tbl_7': tbl_7, 'tbl_8': tbl_8, 'tbl_9': tbl_9, 'tbl_10': tbl_10, 'tbl_11': tbl_11, 'tbl_12': tbl_12, 'tbl_13': tbl_13, 'tbl_14': tbl_14, 'tbl_15': tbl_15, 'tbl_16': tbl_16, 'tbl_17': tbl_17, 'tbl_18': tbl_18, 'tbl_19': tbl_19, 'tbl_20': tbl_20, 'tbl_21': tbl_21, 'tbl_22': tbl_22, 'tbl_23': tbl_23, 'tbl_24': tbl_24, 'tbl_25': tbl_25, 'W_top1': W_top1, 'b_top1': b_top1, 'W_top2': W_top2, 'b_top2': b_top2, 'W_top3': W_top3}

def reference(r_dense_features, ids, tbl_0, tbl_1, tbl_2, tbl_3, tbl_4, tbl_5, tbl_6, tbl_7, tbl_8, tbl_9, tbl_10, tbl_11, tbl_12, tbl_13, tbl_14, tbl_15, tbl_16, tbl_17, tbl_18, tbl_19, tbl_20, tbl_21, tbl_22, tbl_23, tbl_24, tbl_25, W_top1, b_top1, W_top2, b_top2, W_top3):
    import jax
    import jax.numpy as jnp

    def _L0_rec_ref(dense_features, sparse_features):
        import jax, jax.numpy as jnp
        import numpy as np
        NUM_SPARSE = 26
        EMBED_DIM = 128
        BATCH = 2048
        F = NUM_SPARSE + 1
        combined = jnp.concatenate([dense_features[:, None, :], sparse_features], axis=1)
        interactions = jnp.einsum('bfd,bgd->bfg', combined, combined)
        iu, ju = jnp.triu_indices(F, k=1)
        interactions_flat = interactions[:, iu, ju]
        return jnp.concatenate([dense_features, interactions_flat], axis=1)
    e = jnp.stack([tbl_0[ids[:, 0]], tbl_1[ids[:, 1]], tbl_2[ids[:, 2]], tbl_3[ids[:, 3]], tbl_4[ids[:, 4]], tbl_5[ids[:, 5]], tbl_6[ids[:, 6]], tbl_7[ids[:, 7]], tbl_8[ids[:, 8]], tbl_9[ids[:, 9]], tbl_10[ids[:, 10]], tbl_11[ids[:, 11]], tbl_12[ids[:, 12]], tbl_13[ids[:, 13]], tbl_14[ids[:, 14]], tbl_15[ids[:, 15]], tbl_16[ids[:, 16]], tbl_17[ids[:, 17]], tbl_18[ids[:, 18]], tbl_19[ids[:, 19]], tbl_20[ids[:, 20]], tbl_21[ids[:, 21]], tbl_22[ids[:, 22]], tbl_23[ids[:, 23]], tbl_24[ids[:, 24]], tbl_25[ids[:, 25]]], axis=1)
    z = _L0_rec_ref(r_dense_features, e)
    z = z.reshape(z.shape[0], -1)
    h = jnp.concatenate([z, r_dense_features], axis=1)
    h = jnp.maximum(h @ W_top1 + b_top1, 0.0)
    h = jnp.maximum(h @ W_top2 + b_top2, 0.0)
    y = h @ W_top3
    return y

_drawn_inputs = setup_inputs


def setup_inputs(seed=0):
    import zlib

    import numpy as np

    out = dict(_drawn_inputs(seed))
    spreads = {'b_top1': (0.0, 0.1), 'b_top2': (0.0, 0.1)}
    factors = {}
    for name, (base, spread) in spreads.items():
        noise = np.random.default_rng([zlib.crc32(name.encode()), seed]).standard_normal(out[name].shape)
        drawn = base * np.exp(spread * noise) if base else spread * noise
        out[name] = jnp.asarray(drawn.astype(out[name].dtype))
    for name, factor in factors.items():
        out[name] = (out[name] * factor).astype(out[name].dtype)
    return out
```

```python
import concourse.bass as bass
from concourse import mybir
from contextlib import ExitStack

BATCH = 512
D = 128
P = 128
ROWS = [125000, 1250, 1250, 12500, 1250, 12500, 12500, 1000, 1250, 1250, 12500, 1250, 12500,
        12500, 1000, 12500, 1250, 1000, 1250, 1000, 1000, 12500, 1000, 1000, 1000, 1000]
NUM_SPARSE = len(ROWS)
F = NUM_SPARSE + 1
H1, H2 = 512, 256
NT = BATCH // P

ONE_HOT = [7, 14, 17, 19, 20, 22, 23, 24, 25, 1]
GATHERED = [i for i in range(NUM_SPARSE) if i not in ONE_HOT]
KR = 125
CHUNKS = [ROWS[i] // KR for i in ONE_HOT]
MAXC = max(CHUNKS)
GROUPS = [GATHERED[i:i + 4] for i in range(0, len(GATHERED), 4)]
NG = len(GATHERED)

Q = 32
SLOTS = 7
SLOT_ROWS = [sum(1 + SLOTS * j + c < F for j in range(4)) * Q for c in range(SLOTS)]
HALF = 16

TABLE_RING = 5
OH_RING = 5


def pair_rows():
    row = D
    for f in range(F):
        for g in range(f + 1, F):
            yield Q * ((g - 1) // SLOTS) + f, (g - 1) % SLOTS, row
            row += 1


def dlrm_tower(nc, dense_t, idx_dram, oh_ids, tables, w_pairs, w_dense, b1_dram, w2_dram, b2_dram, w3_dram, out):
    fp32 = mybir.dt.float32
    i32 = mybir.dt.int32
    ALU = mybir.AluOpType
    ACT = mybir.ActivationFunctionType

    ctx = ExitStack()
    with ctx:
        def sb(name, shape, dt=fp32):
            return ctx.enter_context(nc.sbuf_tensor(name, shape, dt))

        def sem(name):
            return ctx.enter_context(nc.semaphore(name))

        idx = sb("idx", [P, NT, NUM_SPARSE], i32)
        rows = sb("rows", [P, NT, NG, D])
        table = sb("table", [P, TABLE_RING, MAXC * D])
        ids_all = sb("ids_all", [P, TABLE_RING, BATCH], i32)
        one_hot = sb("one_hot", [P, OH_RING, BATCH])
        row_no_i = sb("row_no_i", [P, 2, MAXC], i32)
        row_no = sb("row_no", [P, 2, MAXC])
        ident = sb("ident", [P, P])
        e_t = sb("e_t", [D, BATCH, Q])
        dense = sb("dense", [D, BATCH])
        z = sb("z", [P, SLOTS, BATCH])
        wp = sb("wp", [P, SLOTS, H1])
        wd2 = sb("wd2", [P, 2, H1])
        wd = sb("wd", [P, H1])
        w2 = sb("w2", [P, H1 // P, H2])
        w3 = sb("w3", [P, H2 // P])
        b1 = sb("b1", [P, H1 // P])
        b2 = sb("b2", [P, H2 // P])
        h1 = sb("h1", [P, H1 // P, P])
        h2 = sb("h2", [P, H2 // P, P])
        y = sb("y", [1, BATCH])

        ps = ctx.enter_context(nc.psum_tensor("ps", [P, 8 * 512], fp32))
        bank = ps[:, :].rearrange("p (k n) -> p k n", k=8)
        gram = ps[:, :].rearrange("p (t n) -> p t n", n=P)

        idx_in = sem("idx_in")
        dense_in = sem("dense_in")
        ids_in = [sem(f"ids_in{i}") for i in range(TABLE_RING)]
        table_in = [sem(f"table_in{i}") for i in range(TABLE_RING)]
        w_in = sem("w_in")
        wd_in = sem("wd_in")
        rows_in = [[sem(f"rows_in{t}_{q}") for q in range(len(GROUPS))] for t in range(NT)]
        cleared = sem("cleared")
        ident_ready = sem("ident_ready")
        iota_ready = sem("iota_ready")
        row_no_ready = sem("row_no_ready")
        pad_ready = sem("pad_ready")
        dense_ready = sem("dense_ready")
        wd_ready = sem("wd_ready")
        one_hot_ready = sem("one_hot_ready")
        one_hot_used = sem("one_hot_used")
        transposed = sem("transposed")
        kept_act = sem("kept_act")
        kept_dve = sem("kept_dve")
        gram_done = sem("gram_done")
        z_act = sem("z_act")
        z_dve = sem("z_dve")
        h1_done = sem("h1_done")
        h1_act = sem("h1_act")
        h1_dve = sem("h1_dve")
        h2_done = sem("h2_done")
        h2_act = sem("h2_act")
        h2_dve = sem("h2_dve")
        y_done = sem("y_done")
        y_kept = sem("y_kept")
        stored = sem("stored")

        jobs = [("table", k, None) for k in range(len(ONE_HOT))]
        jobs += [("group", t, q) for t in range(NT) for q in range(len(GROUPS))]

        def by_act(job):
            return job[0] == "table" or job[2] % 2 == 0

        def wait_kept(eng, n):
            a = sum(by_act(j) for j in jobs[:n])
            if a:
                eng.wait_ge(kept_act, a)
            if n - a:
                eng.wait_ge(kept_dve, n - a)

        def job_no(t, q):
            return len(ONE_HOT) + t * len(GROUPS) + q

        def keep_group(copy, t, q, n):
            src = bank[:, 4 + n % 2, :].rearrange("p (f b) -> p f b", f=4)
            feats = [f + 1 for f in GROUPS[q]]
            runs, i = [], 0
            while i < len(feats):
                m = 1
                step = feats[i + 1] - feats[i] if i + 1 < len(feats) else 1
                while i + m < len(feats) and feats[i + m] - feats[i + m - 1] == step:
                    m += 1
                runs.append((i, m, step))
                i += m
            for i, m, step in runs:
                f0 = feats[i]
                dst = e_t[:, t * P:(t + 1) * P, f0:f0 + step * (m - 1) + 1:step].rearrange("p b f -> p f b")
                last = copy(dst, src[:, i:i + m, :])
            return last

        def take_interactions(copy, t, h, quarters):
            for s in quarters:
                b0 = t * P + 4 * HALF * h + s
                for j in range(4):
                    n = min(SLOTS, F - 1 - SLOTS * j)
                    g0 = F * s + 1 + SLOTS * j
                    last = copy(z[Q * j:Q * (j + 1), 0:n, b0:b0 + 4 * HALF - 3:4].rearrange("p c t -> p t c"),
                                gram[Q * s:Q * (s + 1), HALF * h:HALF * (h + 1), g0:g0 + n])
            return last

        block = ctx.enter_context(nc.Block())

        @block.sync
        def _(sp):
            sp.dma_start(idx[:], idx_dram).then_inc(idx_in, 16)
            for k, f in enumerate(ONE_HOT):
                slot = k % TABLE_RING
                if k >= TABLE_RING:
                    sp.wait_ge(one_hot_used, sum(CHUNKS[:k - TABLE_RING + 1]))
                sp.dma_start(ids_all[:, slot, :], oh_ids[k:k + 1, :].partition_broadcast(P)
                             ).then_inc(ids_in[slot], 16)
                src = tables[f].rearrange("(p c) d -> p (c d)", p=KR)
                sp.dma_start(table[0:112, slot, 0:CHUNKS[k] * D], src[0:112, :]).then_inc(table_in[slot], 16)
                sp.dma_start(table[112:KR, slot, 0:CHUNKS[k] * D], src[112:KR, :]).then_inc(table_in[slot], 16)
                if k == 0:
                    sp.dma_start(dense[:], dense_t).then_inc(dense_in, 16)
                if k == 2:
                    sp.dma_start(wd2[:], w_dense).then_inc(wd_in, 16)
                if k == 3:
                    sp.dma_start(wp[:], w_pairs).then_inc(w_in, 16)
                    sp.dma_start(w2[:], w2_dram).then_inc(w_in, 16)
                    sp.dma_start(w3[:], w3_dram).then_inc(w_in, 16)
                    sp.dma_start(b1[:], b1_dram).then_inc(w_in, 16)
                    sp.dma_start(b2[:], b2_dram).then_inc(w_in, 16)
            sp.wait_ge(y_kept, NT)
            sp.dma_start(out, y[:]).then_inc(stored, 16)
            sp.wait_ge(stored, 16)

        @block.gpsimd
        def _(pool):
            for i, c in enumerate((8, 10)):
                nc.gpsimd.iota(row_no_i[:, i, 0:c], pattern=[[1, c]], base=0, channel_multiplier=c
                               ).then_inc(iota_ready, 1)
            nc.gpsimd.memset(ident[:], 0.0).then_inc(cleared, 1)
            pool.wait_ge(cleared, 1)
            nc.gpsimd.affine_select(out=ident[:], in_=ident[:], compare_op=ALU.not_equal, fill=1.0, base=0,
                                    pattern=[[-1, P]], channel_multiplier=1).then_inc(ident_ready, 1)
            pool.wait_ge(idx_in, 16)
            for t in range(NT):
                for n, f in enumerate(GATHERED):
                    nc.gpsimd.indirect_dma_start(
                        out=rows[:, t, n, :], out_offset=None, in_=tables[f],
                        in_offset=bass.IndirectOffsetOnAxis(ap=idx[:, t, f:f + 1], axis=0),
                    ).then_inc(rows_in[t][n // 4], 16)

        @block.vector
        def _(dve):
            nc.vector.memset(e_t[:, :, F:Q], 0.0).then_inc(pad_ready, 1)
            dve.wait_ge(iota_ready, 2)
            for i, c in enumerate((8, 10)):
                nc.vector.tensor_copy(row_no[:, i, 0:c], row_no_i[:, i, 0:c]).then_inc(row_no_ready, 1)
            dve.wait_ge(row_no_ready, 2)
            n = 0
            for k in range(len(ONE_HOT)):
                slot = k % TABLE_RING
                dve.wait_ge(ids_in[slot], 16 * (k // TABLE_RING + 1))
                kind = (8, 10).index(CHUNKS[k])
                for c in range(CHUNKS[k]):
                    if n >= OH_RING:
                        dve.wait_ge(one_hot_used, n - OH_RING + 1)
                    nc.vector.tensor_scalar(one_hot[0:KR, n % OH_RING, :], ids_all[0:KR, slot, :],
                                            row_no[0:KR, kind, c:c + 1], None, ALU.is_equal
                                            ).then_inc(one_hot_ready, 1)
                    n += 1
                if k == 4:
                    dve.wait_ge(wd_in, 16)
                    nc.vector.tensor_tensor(wd[:], wd2[:, 0, :], wd2[:, 1, :], ALU.add).then_inc(wd_ready, 1)
            for t in range(NT):
                for q in range(len(GROUPS)):
                    n = job_no(t, q)
                    if not by_act(jobs[n]):
                        dve.wait_ge(transposed, n - len(ONE_HOT) + 1)
                        keep_group(nc.vector.tensor_copy, t, q, n).then_inc(kept_dve, 1)
                for h in range(2):
                    dve.wait_ge(gram_done, 2 * t + h + 1)
                    take_interactions(nc.vector.tensor_copy, t, h, (0, 1)).then_inc(z_dve, 1)
                if t == 0:
                    dve.wait_ge(w_in, 16 * 5)
                for n in (1, 3):
                    dve.wait_ge(h1_done, 4 * t + n + 1)
                    nc.vector.tensor_scalar(h1[:, n, :], bank[:, n, 0:P], b1[:, n:n + 1], 0.0, ALU.add, ALU.max
                                            ).then_inc(h1_dve, 1)
                dve.wait_ge(h2_done, 2 * t + 2)
                nc.vector.tensor_scalar(h2[:, 1, :], bank[:, 7, 0:P], b2[:, 1:2], 0.0, ALU.add, ALU.max
                                        ).then_inc(h2_dve, 1)

        @block.scalar
        def _(act):
            act.wait_ge(dense_in, 16)
            nc.scalar.copy(e_t[:, :, 0], dense[:]).then_inc(dense_ready, 1)
            for k, f in enumerate(ONE_HOT):
                act.wait_ge(one_hot_used, sum(CHUNKS[:k + 1]))
                nc.scalar.copy(e_t[:, :, f + 1], bank[:, 4 + k % 2, :]).then_inc(kept_act, 1)
            for t in range(NT):
                for q in range(len(GROUPS)):
                    n = job_no(t, q)
                    if by_act(jobs[n]):
                        act.wait_ge(transposed, n - len(ONE_HOT) + 1)
                        keep_group(nc.scalar.copy, t, q, n).then_inc(kept_act, 1)
                for h in range(2):
                    act.wait_ge(gram_done, 2 * t + h + 1)
                    take_interactions(nc.scalar.copy, t, h, (2, 3)).then_inc(z_act, 1)
                if t == 0:
                    act.wait_ge(w_in, 16 * 5)
                for n in (0, 2):
                    act.wait_ge(h1_done, 4 * t + n + 1)
                    nc.scalar.activation(h1[:, n, :], bank[:, n, 0:P], ACT.Relu, bias=b1[:, n:n + 1]
                                         ).then_inc(h1_act, 1)
                act.wait_ge(h2_done, 2 * t + 1)
                nc.scalar.activation(h2[:, 0, :], bank[:, 6, 0:P], ACT.Relu, bias=b2[:, 0:1]).then_inc(h2_act, 1)
                act.wait_ge(y_done, t + 1)
                nc.scalar.copy(y[0:1, t * P:(t + 1) * P], bank[0:1, 6, P:2 * P]).then_inc(y_kept, 1)

        @block.tensor
        def _(pe):
            n = 0
            for k in range(len(ONE_HOT)):
                slot = k % TABLE_RING
                pe.wait_ge(table_in[slot], 32 * (k // TABLE_RING + 1))
                if k >= 2:
                    wait_kept(pe, k - 1)
                for c in range(CHUNKS[k]):
                    pe.wait_ge(one_hot_ready, n + 1)
                    last = nc.tensor.matmul(bank[:, 4 + k % 2, :], table[0:KR, slot, c * D:(c + 1) * D],
                                            one_hot[0:KR, n % OH_RING, :], start=c == 0, stop=c == CHUNKS[k] - 1)
                    last.then_inc(one_hot_used, 1)
                    n += 1
            pe.wait_ge(ident_ready, 1)
            for t in range(NT):
                for q, feats in enumerate(GROUPS):
                    n = job_no(t, q)
                    pe.wait_ge(rows_in[t][q], 16 * len(feats))
                    wait_kept(pe, n - 1)
                    for i in range(len(feats)):
                        last = nc.tensor.transpose(bank[:, 4 + n % 2, i * P:(i + 1) * P],
                                                   rows[:, t, 4 * q + i, :], ident[:])
                    last.then_inc(transposed, 1)
                wait_kept(pe, job_no(t, len(GROUPS)))
                if t == 0:
                    pe.wait_ge(pad_ready, 1)
                    pe.wait_ge(dense_ready, 1)
                for g in range(P // 4):
                    if g == HALF and t:
                        pe.wait_ge(y_kept, t)
                    feat = e_t[:, t * P + 4 * g:t * P + 4 * g + 4, :]
                    last = nc.tensor.matmul(gram[:, g, 0:4 * F], feat.rearrange("p s f -> p (s f)"), feat[:, :, 0:F], start=True, stop=True)
                    if g % HALF == HALF - 1:
                        last.then_inc(gram_done, 1)
                cols = slice(t * P, (t + 1) * P)
                if t == 0:
                    pe.wait_ge(wd_ready, 1)
                    pe.wait_ge(w_in, 16 * 5)
                pe.wait_ge(z_act, 2 * t + 2)
                pe.wait_ge(z_dve, 2 * t + 2)
                for n in range(H1 // P):
                    out_cols = slice(n * P, (n + 1) * P)
                    nc.tensor.matmul(bank[:, n, 0:P], wd[:, out_cols], dense[:, cols], start=True, stop=False)
                    for c in range(SLOTS):
                        k = SLOT_ROWS[c]
                        last = nc.tensor.matmul(bank[:, n, 0:P], wp[0:k, c, out_cols], z[0:k, c, cols],
                                                start=False, stop=c == SLOTS - 1)
                    last.then_inc(h1_done, 1)
                for m in range(H2 // P):
                    for n in range(H1 // P):
                        if m == 0:
                            if n % 2 == 0:
                                pe.wait_ge(h1_act, 2 * t + n // 2 + 1)
                            else:
                                pe.wait_ge(h1_dve, 2 * t + n // 2 + 1)
                        last = nc.tensor.matmul(bank[:, 6 + m, 0:P], w2[:, n, m * P:(m + 1) * P], h1[:, n, :],
                                                start=n == 0, stop=n == H1 // P - 1)
                    last.then_inc(h2_done, 1)
                pe.wait_ge(h2_act, t + 1)
                nc.tensor.matmul(bank[0:1, 6, P:2 * P], w3[:, 0:1], h2[:, 0, :], start=True, stop=False)
                pe.wait_ge(h2_dve, t + 1)
                nc.tensor.matmul(bank[0:1, 6, P:2 * P], w3[:, 1:2], h2[:, 1, :], start=False, stop=True
                                 ).then_inc(y_done, 1)


def kernel(**inputs):
    import numpy as np
    import concourse.bacc as bacc
    from concourse.bass_utils import run_bass_kernel_spmd

    ids = np.asarray(inputs["ids"])
    w1 = np.asarray(inputs["W_top1"])
    pairs = D + F * (F - 1) // 2
    w_pairs = np.zeros((P, SLOTS, H1), w1.dtype)
    for p, c, row in pair_rows():
        w_pairs[p, c] = w1[row]
    laid_out = {
        "dense_t": np.asarray(inputs["r_dense_features"]).T,
        "idx": ids.reshape(NT, P, NUM_SPARSE).transpose(1, 0, 2),
        "oh_ids": ids.T[ONE_HOT],
        "w_pairs": w_pairs,
        "w_dense": np.stack([w1[0:D], w1[pairs:pairs + D]], axis=1),
        "b1": np.asarray(inputs["b_top1"]).reshape(H1 // P, P).T,
        "w2": np.asarray(inputs["W_top2"]).reshape(H1 // P, P, H2).transpose(1, 0, 2),
        "b2": np.asarray(inputs["b_top2"]).reshape(H2 // P, P).T,
        "w3": np.asarray(inputs["W_top3"]).reshape(H2 // P, P).T,
    }
    laid_out.update({f"tbl_{i}": inputs[f"tbl_{i}"] for i in range(NUM_SPARSE)})

    nc = bacc.Bacc("TRN2", target_bir_lowering=False, num_devices=1)
    arrays, dram = {}, {}
    for name, a in laid_out.items():
        a = np.ascontiguousarray(a)
        arrays[f"in_{name}"] = a
        dram[name] = nc.dram_tensor(f"in_{name}", a.shape, mybir.dt.from_np(a.dtype), kind="ExternalInput").ap()
    out = nc.dram_tensor("out_y", (1, BATCH), mybir.dt.float32, kind="ExternalOutput").ap()
    dlrm_tower(nc, dram["dense_t"], dram["idx"], dram["oh_ids"], [dram[f"tbl_{i}"] for i in range(NUM_SPARSE)],
               dram["w_pairs"], dram["w_dense"], dram["b1"], dram["w2"], dram["b2"], dram["w3"], out)
    result = run_bass_kernel_spmd(nc, [arrays], core_ids=[0])
    return result.results[0]["out_y"].reshape(BATCH, 1)
```

```python
import concourse.bass as bass
from concourse import mybir
from contextlib import ExitStack

BATCH = 512
D = 128
P = 128
ROWS = [125000, 1250, 1250, 12500, 1250, 12500, 12500, 1000, 1250, 1250, 12500, 1250, 12500,
        12500, 1000, 12500, 1250, 1000, 1250, 1000, 1000, 12500, 1000, 1000, 1000, 1000]
NUM_SPARSE = len(ROWS)
F = NUM_SPARSE + 1
H1, H2 = 512, 256
NT = BATCH // P

ONE_HOT = [7, 14, 17, 19, 20, 22, 23]
GATHERED = [i for i in range(NUM_SPARSE) if i not in ONE_HOT]
ORDER = [0] + [i + 1 for i in ONE_HOT + GATHERED]
G0 = 1 + len(ONE_HOT)
KR = 125
CHUNKS = [ROWS[i] // KR for i in ONE_HOT]
MAXC = max(CHUNKS)
KINDS = sorted(set(CHUNKS))
GROUPS = [GATHERED[i:i + 4] for i in range(0, len(GATHERED), 4)]
NG = len(GATHERED)

Q = 32
SLOTS = 7
SLOT_ROWS = [sum(1 + SLOTS * j + c < F for j in range(4)) * Q for c in range(SLOTS)]
HALF = 16

TABLE_RING = 3
IDS_RING = 3
OH_RING = 5


def pair_rows():
    row = D
    for a in range(F):
        for b in range(a + 1, F):
            f, g = sorted((ORDER.index(a), ORDER.index(b)))
            yield Q * ((g - 1) // SLOTS) + f, (g - 1) % SLOTS, row
            row += 1


def dlrm_tower(nc, dense_t, idx_dram, oh_ids, tables, w_pairs, w_dense, b1_dram, w2_dram, b2_dram, w3_dram, out):
    fp32 = mybir.dt.float32
    f32r = mybir.dt.float32r
    i32 = mybir.dt.int32
    ALU = mybir.AluOpType
    ACT = mybir.ActivationFunctionType

    ctx = ExitStack()
    with ctx:
        def sb(name, shape, dt=fp32):
            return ctx.enter_context(nc.sbuf_tensor(name, shape, dt))

        def sem(name):
            return ctx.enter_context(nc.semaphore(name))

        idx = sb("idx", [P, NT, NUM_SPARSE], i32)
        rows = sb("rows", [P, 2, NG, D])
        table = sb("table", [P, TABLE_RING, MAXC * D])
        table_hi = sb("table_hi", [P, 2, MAXC * D], f32r)
        table_lo = sb("table_lo", [P, 2, MAXC * D], f32r)
        ids_all = sb("ids_all", [P, IDS_RING, BATCH], i32)
        one_hot = sb("one_hot", [P, OH_RING, BATCH], f32r)
        row_no_i = sb("row_no_i", [P, len(KINDS), MAXC], i32)
        row_no = sb("row_no", [P, len(KINDS), MAXC])
        ident = sb("ident", [P, P])
        e_t = sb("e_t", [D, BATCH, Q])
        dense = sb("dense", [D, BATCH])
        z = sb("z", [P, SLOTS, P])
        wp = sb("wp", [P, SLOTS, H1])
        wd = sb("wd", [P, H1])
        w2 = sb("w2", [P, H1 // P, H2])
        w3 = sb("w3", [P, H2 // P])
        b1 = sb("b1", [P, H1 // P])
        b2 = sb("b2", [P, H2 // P])
        h1 = sb("h1", [P, H1 // P, P])
        h2 = sb("h2", [P, H2 // P, P])
        y = table[0:1, 0, 0:BATCH]

        ps = ctx.enter_context(nc.psum_tensor("ps", [P, 8 * 512], fp32))
        bank = ps[:, :].rearrange("p (k n) -> p k n", k=8)
        gram = ps[:, :].rearrange("p (t n) -> p t n", n=P)

        idx_in = sem("idx_in")
        dense_in = sem("dense_in")
        ids_in = [sem(f"ids_in{i}") for i in range(IDS_RING)]
        table_in = [sem(f"table_in{i}") for i in range(TABLE_RING)]
        w_in = sem("w_in")
        wd_in = sem("wd_in")
        rows_in = [[sem(f"rows_in{t}_{q}") for q in range(len(GROUPS))] for t in range(NT)]
        cleared = sem("cleared")
        ident_ready = sem("ident_ready")
        iota_ready = sem("iota_ready")
        row_no_ready = sem("row_no_ready")
        pad_ready = sem("pad_ready")
        dense_ready = sem("dense_ready")
        wd_ready = sem("wd_ready")
        hi_ready = sem("hi_ready")
        lo_ready = sem("lo_ready")
        one_hot_ready = sem("one_hot_ready")
        one_hot_used = sem("one_hot_used")
        transposed = sem("transposed")
        table_kept = sem("table_kept")
        kept_act = sem("kept_act")
        kept_dve = sem("kept_dve")
        gram_done = sem("gram_done")
        z_act = sem("z_act")
        z_dve = sem("z_dve")
        h1_done = sem("h1_done")
        h1_act = sem("h1_act")
        h1_dve = sem("h1_dve")
        h2_done = sem("h2_done")
        h2_act = sem("h2_act")
        h2_dve = sem("h2_dve")
        y_done = sem("y_done")
        y_kept = sem("y_kept")
        stored = sem("stored")

        def wait_groups(eng, n):
            eng.wait_ge(kept_act, (n + 1) // 2)
            if n >= 2:
                eng.wait_ge(kept_dve, n // 2)

        def group_places(t, q):
            f = G0 + 4 * q
            return e_t[:, t * P:(t + 1) * P, f:f + len(GROUPS[q])].rearrange("p b f -> p f b")

        def group_bank(t, q):
            n = (t * len(GROUPS) + q) % 2
            return bank[:, 4 + n, 0:P * len(GROUPS[q])].rearrange("p (f b) -> p f b", b=P)

        def take_interactions(copy, t, h, quarters):
            for s in quarters:
                b0 = 4 * HALF * h + s
                for j in range(4):
                    n = min(SLOTS, F - 1 - SLOTS * j)
                    g0 = F * s + 1 + SLOTS * j
                    last = copy(z[Q * j:Q * (j + 1), 0:n, b0:b0 + 4 * HALF - 3:4].rearrange("p c t -> p t c"),
                                gram[Q * s:Q * (s + 1), HALF * h:HALF * (h + 1), g0:g0 + n])
            return last

        block = ctx.enter_context(nc.Block())

        @block.sync
        def _(sp):
            sp.dma_start(idx[:], idx_dram).then_inc(idx_in, 16)
            for k, f in enumerate(ONE_HOT):
                slot = k % TABLE_RING
                if k >= TABLE_RING:
                    sp.wait_ge(hi_ready, k - TABLE_RING + 1)
                    sp.wait_ge(lo_ready, k - TABLE_RING + 1)
                src = tables[f].rearrange("(p c) d -> p (c d)", p=KR)
                sp.dma_start(table[0:112, slot, 0:CHUNKS[k] * D], src[0:112, :]).then_inc(table_in[slot], 16)
                sp.dma_start(table[112:KR, slot, 0:CHUNKS[k] * D], src[112:KR, :]).then_inc(table_in[slot], 16)
                if k >= IDS_RING:
                    sp.wait_ge(one_hot_ready, sum(CHUNKS[:k - IDS_RING + 1]))
                sp.dma_start(ids_all[:, k % IDS_RING, :], oh_ids[k:k + 1, :].partition_broadcast(P)
                             ).then_inc(ids_in[k % IDS_RING], 16)
                if k == 0:
                    sp.dma_start(dense[:], dense_t).then_inc(dense_in, 16)
                if k == 2:
                    sp.dma_start(wd[:], w_dense[:, 0, :]).then_inc(wd_in, 16)
                    sp.dma_start(h1[:].rearrange("p n b -> p (n b)"), w_dense[:, 1, :]).then_inc(wd_in, 16)
                if k == 3:
                    sp.dma_start(wp[:], w_pairs).then_inc(w_in, 16)
                    sp.dma_start(w2[:], w2_dram).then_inc(w_in, 16)
                    sp.dma_start(w3[:], w3_dram).then_inc(w_in, 16)
                    sp.dma_start(b1[:], b1_dram).then_inc(w_in, 16)
                    sp.dma_start(b2[:], b2_dram).then_inc(w_in, 16)
            sp.wait_ge(y_kept, NT)
            sp.dma_start(out, y).then_inc(stored, 16)
            sp.wait_ge(stored, 16)

        @block.gpsimd
        def _(pool):
            for i, c in enumerate(KINDS):
                nc.gpsimd.iota(row_no_i[:, i, 0:c], pattern=[[1, c]], base=0, channel_multiplier=c
                               ).then_inc(iota_ready, 1)
            nc.gpsimd.memset(ident[:], 0.0).then_inc(cleared, 1)
            pool.wait_ge(cleared, 1)
            nc.gpsimd.affine_select(out=ident[:], in_=ident[:], compare_op=ALU.not_equal, fill=1.0, base=0,
                                    pattern=[[-1, P]], channel_multiplier=1).then_inc(ident_ready, 1)
            pool.wait_ge(idx_in, 16)
            for t in range(NT):
                for n, f in enumerate(GATHERED):
                    if t >= 2 and n % 4 == 0:
                        pool.wait_ge(transposed, (t - 2) * len(GROUPS) + n // 4 + 1)
                    nc.gpsimd.indirect_dma_start(
                        out=rows[:, t % 2, n, :], out_offset=None, in_=tables[f],
                        in_offset=bass.IndirectOffsetOnAxis(ap=idx[:, t, f:f + 1], axis=0),
                    ).then_inc(rows_in[t][n // 4], 16)

        @block.vector
        def _(dve):
            nc.vector.memset(e_t[:, :, F:Q], 0.0).then_inc(pad_ready, 1)
            dve.wait_ge(iota_ready, len(KINDS))
            for i, c in enumerate(KINDS):
                nc.vector.tensor_copy(row_no[:, i, 0:c], row_no_i[:, i, 0:c]).then_inc(row_no_ready, 1)
            dve.wait_ge(row_no_ready, len(KINDS))
            n = 0
            for k in range(len(ONE_HOT)):
                slot = k % TABLE_RING
                dve.wait_ge(ids_in[k % IDS_RING], 16 * (k // IDS_RING + 1))
                kind = KINDS.index(CHUNKS[k])
                width = CHUNKS[k] * D
                dve.wait_ge(hi_ready, k + 1)
                if k >= 2:
                    dve.wait_ge(one_hot_used, sum(CHUNKS[:k - 1]))
                nc.vector.tensor_tensor(table_lo[0:KR, k % 2, 0:width], table[0:KR, slot, 0:width],
                                        table_hi[0:KR, k % 2, 0:width].bitcast(fp32), ALU.subtract
                                        ).then_inc(lo_ready, 1)
                for c in range(CHUNKS[k]):
                    if n >= OH_RING:
                        dve.wait_ge(one_hot_used, n - OH_RING + 1)
                    nc.vector.tensor_scalar(one_hot[0:KR, n % OH_RING, :], ids_all[0:KR, k % IDS_RING, :],
                                            row_no[0:KR, kind, c:c + 1], None, ALU.is_equal
                                            ).then_inc(one_hot_ready, 1)
                    n += 1
                if k == 4:
                    dve.wait_ge(wd_in, 32)
                    nc.vector.tensor_tensor(wd[:], wd[:], h1[:].rearrange("p n b -> p (n b)"), ALU.add).then_inc(wd_ready, 1)
            for t in range(NT):
                for q in range(len(GROUPS)):
                    n = t * len(GROUPS) + q
                    if n % 2:
                        dve.wait_ge(transposed, n + 1)
                        nc.vector.tensor_copy(group_places(t, q), group_bank(t, q)).then_inc(kept_dve, 1)
                for h in range(2):
                    dve.wait_ge(gram_done, 2 * t + h + 1)
                    take_interactions(nc.vector.tensor_copy, t, h, (0, 1)).then_inc(z_dve, 1)
                if t == 0:
                    dve.wait_ge(w_in, 16 * 5)
                for n in (1, 3):
                    dve.wait_ge(h1_done, 4 * t + n + 1)
                    nc.vector.tensor_scalar(h1[:, n, :], bank[:, n, 0:P], b1[:, n:n + 1], 0.0, ALU.add, ALU.max
                                            ).then_inc(h1_dve, 1)
                dve.wait_ge(h2_done, 2 * t + 2)
                nc.vector.tensor_scalar(h2[:, 1, :], bank[:, 7, 0:P], b2[:, 1:2], 0.0, ALU.add, ALU.max
                                        ).then_inc(h2_dve, 1)

        @block.scalar
        def _(act):
            def keep_table(act, k):
                nc.scalar.copy(e_t[:, :, 1 + k], bank[:, 4 + k % 2, :]).then_inc(table_kept, 1)

            for k in range(len(ONE_HOT)):
                slot = k % TABLE_RING
                width = CHUNKS[k] * D
                act.wait_ge(table_in[slot], 32 * (k // TABLE_RING + 1))
                if k >= 2:
                    act.wait_ge(one_hot_used, sum(CHUNKS[:k - 1]))
                    keep_table(act, k - 2)
                nc.scalar.copy(table_hi[0:KR, k % 2, 0:width], table[0:KR, slot, 0:width]).then_inc(hi_ready, 1)
                if k == 1:
                    act.wait_ge(dense_in, 16)
                    nc.scalar.copy(e_t[:, :, 0], dense[:]).then_inc(dense_ready, 1)
            for k in range(len(ONE_HOT) - 2, len(ONE_HOT)):
                act.wait_ge(one_hot_used, sum(CHUNKS[:k + 1]))
                keep_table(act, k)
            for t in range(NT):
                for q in range(len(GROUPS)):
                    n = t * len(GROUPS) + q
                    if n % 2 == 0:
                        act.wait_ge(transposed, n + 1)
                        nc.scalar.copy(group_places(t, q), group_bank(t, q)).then_inc(kept_act, 1)
                for h in range(2):
                    act.wait_ge(gram_done, 2 * t + h + 1)
                    take_interactions(nc.scalar.copy, t, h, (2, 3)).then_inc(z_act, 1)
                if t == 0:
                    act.wait_ge(w_in, 16 * 5)
                for n in (0, 2):
                    act.wait_ge(h1_done, 4 * t + n + 1)
                    nc.scalar.activation(h1[:, n, :], bank[:, n, 0:P], ACT.Relu, bias=b1[:, n:n + 1]
                                         ).then_inc(h1_act, 1)
                act.wait_ge(h2_done, 2 * t + 1)
                nc.scalar.activation(h2[:, 0, :], bank[:, 6, 0:P], ACT.Relu, bias=b2[:, 0:1]).then_inc(h2_act, 1)
                act.wait_ge(y_done, t + 1)
                nc.scalar.copy(y[:, t * P:(t + 1) * P], bank[0:1, 6, P:2 * P]).then_inc(y_kept, 1)

        @block.tensor
        def _(pe):
            n = 0
            for k in range(len(ONE_HOT)):
                pe.wait_ge(hi_ready, k + 1)
                pe.wait_ge(lo_ready, k + 1)
                if k >= 2:
                    pe.wait_ge(table_kept, k - 1)
                for c in range(CHUNKS[k]):
                    pe.wait_ge(one_hot_ready, n + 1)
                    rows_c = slice(c * D, (c + 1) * D)
                    nc.tensor.matmul(bank[:, 4 + k % 2, :], table_hi[0:KR, k % 2, rows_c],
                                     one_hot[0:KR, n % OH_RING, :], start=c == 0, stop=False)
                    nc.tensor.matmul(bank[:, 4 + k % 2, :], table_lo[0:KR, k % 2, rows_c],
                                     one_hot[0:KR, n % OH_RING, :], start=False, stop=c == CHUNKS[k] - 1
                                     ).then_inc(one_hot_used, 1)
                    n += 1
            pe.wait_ge(ident_ready, 1)
            pe.wait_ge(table_kept, len(ONE_HOT))
            for t in range(NT):
                for q, feats in enumerate(GROUPS):
                    n = t * len(GROUPS) + q
                    pe.wait_ge(rows_in[t][q], 16 * len(feats))
                    if n >= 2:
                        wait_groups(pe, n - 1)
                    for i in range(len(feats)):
                        last = nc.tensor.transpose(group_bank(t, q)[:, i, :], rows[:, t % 2, 4 * q + i, :], ident[:])
                    last.then_inc(transposed, 1)
                wait_groups(pe, (t + 1) * len(GROUPS))
                if t == 0:
                    pe.wait_ge(pad_ready, 1)
                    pe.wait_ge(dense_ready, 1)
                for g in range(P // 4):
                    if g == HALF and t:
                        pe.wait_ge(y_kept, t)
                    four = slice(t * P + 4 * g, t * P + 4 * g + 4)
                    last = nc.tensor.matmul(gram[:, g, 0:4 * F], e_t[:, four, :].rearrange("p s f -> p (s f)"),
                                            e_t[:, four, 0:F], start=True, stop=True)
                    if g % HALF == HALF - 1:
                        last.then_inc(gram_done, 1)
                cols = slice(t * P, (t + 1) * P)
                if t == 0:
                    pe.wait_ge(wd_ready, 1)
                    pe.wait_ge(w_in, 16 * 5)
                pe.wait_ge(z_act, 2 * t + 2)
                pe.wait_ge(z_dve, 2 * t + 2)
                for n in range(H1 // P):
                    out_cols = slice(n * P, (n + 1) * P)
                    nc.tensor.matmul(bank[:, n, 0:P], wd[:, out_cols], dense[:, cols], start=True, stop=False)
                    for c in range(SLOTS):
                        k = SLOT_ROWS[c]
                        last = nc.tensor.matmul(bank[:, n, 0:P], wp[0:k, c, out_cols], z[0:k, c, :],
                                                start=False, stop=c == SLOTS - 1)
                    last.then_inc(h1_done, 1)
                for m in range(H2 // P):
                    for n in range(H1 // P):
                        if m == 0:
                            if n % 2 == 0:
                                pe.wait_ge(h1_act, 2 * t + n // 2 + 1)
                            else:
                                pe.wait_ge(h1_dve, 2 * t + n // 2 + 1)
                        last = nc.tensor.matmul(bank[:, 6 + m, 0:P], w2[:, n, m * P:(m + 1) * P], h1[:, n, :],
                                                start=n == 0, stop=n == H1 // P - 1)
                    last.then_inc(h2_done, 1)
                pe.wait_ge(h2_act, t + 1)
                nc.tensor.matmul(bank[0:1, 6, P:2 * P], w3[:, 0:1], h2[:, 0, :], start=True, stop=False)
                pe.wait_ge(h2_dve, t + 1)
                nc.tensor.matmul(bank[0:1, 6, P:2 * P], w3[:, 1:2], h2[:, 1, :], start=False, stop=True
                                 ).then_inc(y_done, 1)


def kernel(**inputs):
    import numpy as np
    import concourse.bacc as bacc
    from concourse.bass_utils import run_bass_kernel_spmd

    ids = np.asarray(inputs["ids"])
    w1 = np.asarray(inputs["W_top1"])
    pairs = D + F * (F - 1) // 2
    w_pairs = np.zeros((P, SLOTS, H1), w1.dtype)
    for p, c, row in pair_rows():
        w_pairs[p, c] = w1[row]
    laid_out = {
        "dense_t": np.asarray(inputs["r_dense_features"]).T,
        "idx": ids.reshape(NT, P, NUM_SPARSE).transpose(1, 0, 2),
        "oh_ids": ids.T[ONE_HOT],
        "w_pairs": w_pairs,
        "w_dense": np.stack([w1[0:D], w1[pairs:pairs + D]], axis=1),
        "b1": np.asarray(inputs["b_top1"]).reshape(H1 // P, P).T,
        "w2": np.asarray(inputs["W_top2"]).reshape(H1 // P, P, H2).transpose(1, 0, 2),
        "b2": np.asarray(inputs["b_top2"]).reshape(H2 // P, P).T,
        "w3": np.asarray(inputs["W_top3"]).reshape(H2 // P, P).T,
    }
    laid_out.update({f"tbl_{i}": inputs[f"tbl_{i}"] for i in range(NUM_SPARSE)})

    nc = bacc.Bacc("TRN2", target_bir_lowering=False, num_devices=1)
    arrays, dram = {}, {}
    for name, a in laid_out.items():
        a = np.ascontiguousarray(a)
        arrays[f"in_{name}"] = a
        dram[name] = nc.dram_tensor(f"in_{name}", a.shape, mybir.dt.from_np(a.dtype), kind="ExternalInput").ap()
    out = nc.dram_tensor("out_y", (1, BATCH), mybir.dt.float32, kind="ExternalOutput").ap()
    dlrm_tower(nc, dram["dense_t"], dram["idx"], dram["oh_ids"], [dram[f"tbl_{i}"] for i in range(NUM_SPARSE)],
               dram["w_pairs"], dram["w_dense"], dram["b1"], dram["w2"], dram["b2"], dram["w3"], out)
    result = run_bass_kernel_spmd(nc, [arrays], core_ids=[0])
    return result.results[0]["out_y"].reshape(BATCH, 1)
```

```python
import concourse.bass as bass
from concourse import mybir
from contextlib import ExitStack

BATCH = 512
D = 128
P = 128
ROWS = [125000, 1250, 1250, 12500, 1250, 12500, 12500, 1000, 1250, 1250, 12500, 1250, 12500,
        12500, 1000, 12500, 1250, 1000, 1250, 1000, 1000, 12500, 1000, 1000, 1000, 1000]
NUM_SPARSE = len(ROWS)
F = NUM_SPARSE + 1
H1, H2 = 512, 256
NT = BATCH // P

ONE_HOT = [7, 14, 17, 19, 20, 22, 23, 24]
GATHERED = [i for i in range(NUM_SPARSE) if i not in ONE_HOT]
ORDER = [0] + [i + 1 for i in ONE_HOT + GATHERED]
G0 = 1 + len(ONE_HOT)
KR = 125
C = ROWS[ONE_HOT[0]] // KR
GROUPS = [GATHERED[i:i + 4] for i in range(0, len(GATHERED), 4)]
NG = len(GATHERED)
AFTER_QUARTER = [[[2], [3], [4], []], [[], [0], [1], []], [[0, 1], [2], [3], []]]
AFTER_LAYER1 = [[], [2], [3], [4]]

Q = 32
SLOTS = 6
FOLDED = F - 1 - P // Q * SLOTS
G1 = 1 + FOLDED
NQ = 4
QS = P // NQ
PAIR = 2 * P
PARTS = SLOTS + 1
TABLE_RING = 3
SPLIT_RING = 3
OH_RING = 6

EARLY = list(range(len(ONE_HOT) % TABLE_RING * C * D // H1, (len(ONE_HOT) % TABLE_RING + 1) * C * D // H1))
LATE = [c for c in range(SLOTS) if c not in EARLY]
W1_ORDER = EARLY + [SLOTS] + LATE
AHEAD = 4

LAYER2_ORDER = [(0, 0), (1, 0), (2, 0), (0, 1), (1, 1), (3, 0), (2, 1), (3, 1)]

ACT_CHUNKS = [[C - 1] if k % 2 == 0 else [3, C - 1] for k in range(len(ONE_HOT))]


def made_by_act(k, c):
    return sum(map(len, ACT_CHUNKS[:k])) + len([i for i in ACT_CHUNKS[k] if i < c])


def made_by_dve(k, c):
    return C * k + c - made_by_act(k, c)


def pair_rows():
    row = D
    for a in range(F):
        for b in range(a + 1, F):
            f, g = sorted((ORDER.index(a), ORDER.index(b)))
            if g < G1:
                yield F + f, g - 1, row
            else:
                yield Q * ((g - G1) // SLOTS) + f, (g - G1) % SLOTS, row
            row += 1


def dlrm_tower(nc, dense_t, idx_dram, oh_ids, tables, w1_dram, wd_dram, b1_dram, w2_dram, b2_dram, w3_dram, out):
    fp32 = mybir.dt.float32
    f32r = mybir.dt.float32r
    i32 = mybir.dt.int32
    ALU = mybir.AluOpType
    ACT = mybir.ActivationFunctionType

    ctx = ExitStack()
    with ctx:
        def sb(name, shape, dt=fp32):
            return ctx.enter_context(nc.sbuf_tensor(name, shape, dt))

        def sem(name):
            return ctx.enter_context(nc.semaphore(name))

        idx = sb("idx", [P, NT, NUM_SPARSE], i32)
        rows = sb("rows", [P, 2, NG, D])
        space = sb("space", [P, PARTS * H1])
        table = space[:, 0:TABLE_RING * C * D].rearrange("p (r n) -> p r n", r=TABLE_RING)
        w1 = space[:, :].rearrange("p (c n) -> p c n", c=PARTS)
        table_hi = sb("table_hi", [P, SPLIT_RING, C * D], f32r)
        table_lo = sb("table_lo", [P, SPLIT_RING, C * D], f32r)
        ids_all = sb("ids_all", [P, TABLE_RING, BATCH], i32)
        square = sb("square", [P, BATCH])
        one = sb("one", [P, 1])
        one_hot = sb("one_hot", [P, OH_RING, BATCH], f32r)
        row_no_i = sb("row_no_i", [P, C], i32)
        row_no = sb("row_no", [P, C])
        minus_row_no = sb("minus_row_no", [P, C])
        ident = sb("ident", [P, P])
        e_t = sb("e_t", [D, BATCH, Q])
        dense = sb("dense", [D, BATCH])
        dense_hi = sb("dense_hi", [D, BATCH], f32r)
        dense_lo = sb("dense_lo", [D, BATCH], f32r)
        z = sb("z", [P, SLOTS, P])
        z_hi = sb("z_hi", [P, SLOTS, PAIR], f32r)
        z_lo = sb("z_lo", [P, SLOTS, PAIR], f32r)
        w1_hi = sb("w1_hi", [P, PARTS, H1], f32r)
        w1_lo = sb("w1_lo", [P, PARTS, H1], f32r)
        w2 = sb("w2", [P, H1 // P, H2])
        w3 = sb("w3", [P, H2 // P])
        b1 = sb("b1", [P, H1 // P])
        b2 = sb("b2", [P, H2 // P])
        h1 = sb("h1", [P, H1 // P, PAIR])
        w2_hi = table_hi[:, 0, :].rearrange("p (n m) -> p n m", n=H1 // P)
        w2_lo = table_lo[:, 0, :].rearrange("p (n m) -> p n m", n=H1 // P)
        h1_hi = table_hi[:, 1, :].rearrange("p (n b) -> p n b", n=H1 // P)
        h1_lo = table_lo[:, 1, :].rearrange("p (n b) -> p n b", n=H1 // P)
        h2 = square[:, :].rearrange("p (m b) -> p m b", m=H2 // P)
        y = sb("y", [1, BATCH])

        ps = ctx.enter_context(nc.psum_tensor("ps", [P, 8 * 512], fp32))
        bank = ps[:, :].rearrange("p (k n) -> p k n", k=8)
        gram = ps[:, :].rearrange("p (k t n) -> p k t n", k=4, n=P)
        l1_bank = [4, 5, 0, 1]

        idx_in = sem("idx_in")
        dense_in = sem("dense_in")
        ids_in = [sem(f"ids_in{i}") for i in range(TABLE_RING)]
        table_in = [[sem(f"table_in{i}_{h}") for h in range(2)] for i in range(TABLE_RING)]
        w_in = sem("w_in")
        wd_in = sem("wd_in")
        w1_early = sem("w1_early")
        w1_late = sem("w1_late")
        rows_in = [[sem(f"rows_in{t}_{q}") for q in range(len(GROUPS))] for t in range(NT)]
        cleared = sem("cleared")
        ident_ready = sem("ident_ready")
        iota_ready = sem("iota_ready")
        row_no_ready = sem("row_no_ready")
        pad_ready = sem("pad_ready")
        z_cleared = sem("z_cleared")
        copies_ready = sem("copies_ready")
        folded_act = sem("folded_act")
        folded_dve = sem("folded_dve")
        dense_ready = sem("dense_ready")
        dense_hi_ready = sem("dense_hi_ready")
        dense_lo_ready = sem("dense_lo_ready")
        w1_summed = sem("w1_summed")
        w1_hi_ready = sem("w1_hi_ready")
        w1_lo_ready = sem("w1_lo_ready")
        hi_ready = sem("hi_ready")
        lo_ready = sem("lo_ready")
        squared = sem("squared")
        one_hot_dve = sem("one_hot_dve")
        one_hot_act = sem("one_hot_act")
        one_hot_used = sem("one_hot_used")
        transposed = sem("transposed")
        table_kept = sem("table_kept")
        kept_act = sem("kept_act")
        kept_dve = sem("kept_dve")
        gram_done = sem("gram_done")
        z_act = sem("z_act")
        z_dve = sem("z_dve")
        z_hi_act = sem("z_hi_act")
        z_hi_dve = sem("z_hi_dve")
        z_lo_ready = sem("z_lo_ready")
        h1_done = sem("h1_done")
        h1_ready = sem("h1_ready")
        h1_hi_ready = sem("h1_hi_ready")
        h1_lo_ready = sem("h1_lo_ready")
        w2_hi_ready = sem("w2_hi_ready")
        w2_lo_ready = sem("w2_lo_ready")
        h2_done = sem("h2_done")
        h2_act = sem("h2_act")
        h2_dve = sem("h2_dve")
        y_done = sem("y_done")
        y_kept = sem("y_kept")
        stored = sem("stored")

        def half_cols(h):
            return slice(h * C // 2 * D, (h + 1) * C // 2 * D)

        def wait_groups(eng, n):
            eng.wait_ge(kept_act, (n + 1) // 2)
            if n >= 2:
                eng.wait_ge(kept_dve, n // 2)

        def group_places(t, q):
            f = G0 + 4 * q
            return e_t[:, t * P:(t + 1) * P, f:f + len(GROUPS[q])].rearrange("p b f -> p f b")

        def group_bank(t, q):
            if t == 0:
                k = q
            elif (t, q) == (1, 0):
                k = 5
            else:
                k = 6 + (t * len(GROUPS) + q - (len(GROUPS) + 1) + len(ONE_HOT)) % 2
            return bank[:, k, 0:P * len(GROUPS[q])].rearrange("p (f b) -> p f b", b=P)

        def take_interactions(copy, eng, folded, t, q, quadrants):
            i = NQ * t + q
            two_banks = gram[:, i % (2 * NQ) % 3, :, :]

            def take(s, j, rows, g0, n):
                b0 = QS * q + s
                return copy(z[Q * j:Q * j + rows, 0:n, b0:b0 + QS - 3:4].rearrange("p c t -> p t c"),
                            two_banks[Q * s:Q * s + rows, :, F * s + g0:F * s + g0 + n])

            for s in quadrants:
                take(s, 0, Q, 1, FOLDED).then_inc(folded, 1)
            for s in quadrants:
                for j in range(1, 4):
                    take(s, j, Q, G1 + SLOTS * j, SLOTS)
            if i == 0:
                eng.wait_ge(z_cleared, 1)
            eng.wait_ge(folded, len(quadrants) * (i + 1))
            for s in quadrants:
                last = take(s, 0, F, G1, SLOTS)
            return last

        def z_quarter(array, t, q, s0, s1):
            b0 = QS * q + (0 if array is z else t % 2 * P)
            return array[:, :, b0:b0 + QS].rearrange("p c (g s) -> p c g s", s=4)[:, :, :, s0:s1]

        block = ctx.enter_context(nc.Block())

        @block.sync
        def _(sp):
            sp.dma_start(idx[:], idx_dram).then_inc(idx_in, 16)
            for k, f in enumerate(ONE_HOT):
                slot = k % TABLE_RING
                src = tables[f].rearrange("(p c) d -> p (c d)", p=KR)
                if k >= TABLE_RING:
                    sp.wait_ge(one_hot_dve, made_by_dve(k - TABLE_RING + 1, 0))
                    sp.wait_ge(one_hot_act, made_by_act(k - TABLE_RING + 1, 0))
                sp.dma_start(ids_all[:, slot, :], oh_ids[k:k + 1, :].partition_broadcast(P)).then_inc(ids_in[slot], 16)
                if k >= TABLE_RING:
                    sp.wait_ge(hi_ready, 2 * (k - TABLE_RING + 1))
                    sp.wait_ge(lo_ready, 2 * (k - TABLE_RING + 1))
                for h in range(2):
                    cols = half_cols(h)
                    sp.dma_start(table[0:112, slot, cols], src[0:112, cols]).then_inc(table_in[slot][h], 16)
                    sp.dma_start(table[112:KR, slot, cols], src[112:KR, cols]).then_inc(table_in[slot][h], 16)
                if k == 0:
                    sp.dma_start(dense[:], dense_t).then_inc(dense_in, 16)
            sp.dma_start(w2[:], w2_dram).then_inc(w_in, 16)
            sp.dma_start(w3[:], w3_dram).then_inc(w_in, 16)
            sp.dma_start(b1[:], b1_dram).then_inc(w_in, 16)
            sp.dma_start(b2[:], b2_dram).then_inc(w_in, 16)
            sp.dma_start(w1[:, SLOTS, :], wd_dram[0]).then_inc(wd_in, 16)
            sp.dma_start(h1[:, 0:2, :].rearrange("p n b -> p (n b)"), wd_dram[1]).then_inc(wd_in, 16)
            sp.wait_ge(hi_ready, 2 * (len(ONE_HOT) - 2))
            sp.wait_ge(lo_ready, 2 * (len(ONE_HOT) - 2))
            sp.dma_start(w1[:, EARLY[0]:EARLY[-1] + 1, :], w1_dram[:, EARLY[0]:EARLY[-1] + 1, :]).then_inc(w1_early, 16)
            sp.wait_ge(hi_ready, 2 * len(ONE_HOT))
            sp.wait_ge(lo_ready, 2 * len(ONE_HOT))
            sp.dma_start(w1[:, LATE[0]:LATE[-1] + 1, :], w1_dram[:, LATE[0]:LATE[-1] + 1, :]).then_inc(w1_late, 16)
            sp.wait_ge(y_kept, NT // 2)
            sp.dma_start(out, y[:]).then_inc(stored, 16)
            sp.wait_ge(stored, 16)

        @block.gpsimd
        def _(pool):
            nc.gpsimd.iota(row_no_i[:], pattern=[[1, C]], base=0, channel_multiplier=C).then_inc(iota_ready, 1)
            nc.gpsimd.memset(ident[:], 0.0).then_inc(cleared, 1)
            pool.wait_ge(cleared, 1)
            nc.gpsimd.affine_select(out=ident[:], in_=ident[:], compare_op=ALU.not_equal, fill=1.0, base=0,
                                    pattern=[[-1, P]], channel_multiplier=1).then_inc(ident_ready, 1)
            pool.wait_ge(idx_in, 16)
            for t in range(NT):
                for n, f in enumerate(GATHERED):
                    if t >= 2 and n % 4 == 0:
                        pool.wait_ge(transposed, (t - 2) * len(GROUPS) + n // 4 + 1)
                    nc.gpsimd.indirect_dma_start(
                        out=rows[:, t % 2, n, :], out_offset=None, in_=tables[f],
                        in_offset=bass.IndirectOffsetOnAxis(ap=idx[:, t, f:f + 1], axis=0),
                    ).then_inc(rows_in[t][n // 4], 16)

        @block.vector
        def _(dve):
            nc.vector.memset(e_t[:, :, F + FOLDED:Q], 0.0).then_inc(pad_ready, 1)
            nc.vector.memset(z[0:Q, FOLDED:SLOTS, :], 0.0).then_inc(z_cleared, 1)
            dve.wait_ge(iota_ready, 1)
            nc.vector.tensor_copy(row_no[:], row_no_i[:]).then_inc(row_no_ready, 1)
            nc.vector.tensor_scalar(minus_row_no[:], row_no_i[:], -1.0, None, ALU.mult).then_inc(row_no_ready, 1)
            nc.vector.memset(one[:], 1.0).then_inc(row_no_ready, 1)
            dve.wait_ge(row_no_ready, 3)

            def table_rest(k, h):
                cols = half_cols(h)
                dve.wait_ge(hi_ready, 2 * k + h + 1)
                if k >= SPLIT_RING:
                    dve.wait_ge(one_hot_used, C * (k - SPLIT_RING + 1))
                nc.vector.tensor_tensor(table_lo[0:KR, k % SPLIT_RING, cols], table[0:KR, k % TABLE_RING, cols],
                                        table_hi[0:KR, k % SPLIT_RING, cols].bitcast(fp32), ALU.subtract
                                        ).then_inc(lo_ready, 1)

            for k in range(len(ONE_HOT)):
                for c in range(C):
                    if k == 0 and c == 3:
                        table_rest(0, 0)
                    if c == 3 + int(k == 0):
                        table_rest(k, 1)
                    if c == C - 1 and k + 1 < len(ONE_HOT):
                        table_rest(k + 1, 0)
                    if c in ACT_CHUNKS[k]:
                        continue
                    if c == 0:
                        dve.wait_ge(ids_in[k % TABLE_RING], 16 * (k // TABLE_RING + 1))
                    n = C * k + c
                    if n >= OH_RING:
                        dve.wait_ge(one_hot_used, n - OH_RING + 1)
                    nc.vector.tensor_scalar(one_hot[0:KR, n % OH_RING, :], ids_all[0:KR, k % TABLE_RING, :],
                                            row_no[0:KR, c:c + 1], None, ALU.is_equal).then_inc(one_hot_dve, 1)

            def keep_groups(t, qs):
                for q in qs:
                    n = t * len(GROUPS) + q
                    if n % 2:
                        dve.wait_ge(transposed, n + 1)
                        nc.vector.tensor_copy(group_places(t, q), group_bank(t, q)).then_inc(kept_dve, 1)

            def z_rest(i):
                def quarter(array):
                    return z_quarter(array, i // NQ, i % NQ, 0, 4)

                dve.wait_ge(z_hi_dve, i + 1)
                dve.wait_ge(z_hi_act, i + 1)
                nc.vector.tensor_tensor(quarter(z_lo), quarter(z), quarter(z_hi).bitcast(fp32), ALU.subtract
                                        ).then_inc(z_lo_ready, 1)

            keep_groups(0, range(len(GROUPS)))
            dve.wait_ge(dense_hi_ready, 1)
            nc.vector.tensor_tensor(dense_lo[:], dense[:], dense_hi[:].bitcast(fp32), ALU.subtract
                                    ).then_inc(dense_lo_ready, 1)
            dve.wait_ge(wd_in, 32)
            nc.vector.tensor_tensor(w1[:, SLOTS, :], w1[:, SLOTS, :], h1[:, 0:2, :].rearrange("p n b -> p (n b)"),
                                    ALU.add).then_inc(w1_summed, 1)

            def weights_rest(i):
                c = W1_ORDER[i]
                dve.wait_ge(w1_hi_ready, i + 1)
                nc.vector.tensor_tensor(w1_lo[:, c, :], w1[:, c, :], w1_hi[:, c, :].bitcast(fp32),
                                        ALU.subtract).then_inc(w1_lo_ready, 1)

            keep_groups(1, [0, 1])
            for i in range(AHEAD):
                weights_rest(i)
            for t in range(NT):
                for q in range(NQ):
                    i = NQ * t + q
                    if t == NT - 2 and q == NQ - 1:
                        keep_groups(t + 1, range(4, len(GROUPS)))
                    dve.wait_ge(gram_done, i + 1)
                    if i >= NQ:
                        dve.wait_ge(z_lo_ready, i - NQ + 1)
                    take_interactions(nc.vector.tensor_copy, dve, folded_dve, t, q, (0, 1)).then_inc(z_dve, 1)
                    dve.wait_ge(z_dve, i + 1)
                    nc.vector.tensor_copy(z_quarter(z_hi, t, q, 0, 2), z_quarter(z, t, q, 0, 2)).then_inc(z_hi_dve, 1)
                    if t < NT - 1:
                        keep_groups(t + 1, AFTER_QUARTER[t][q])
                    if q or t % 2:
                        z_rest(i - 1)
                    if q == NQ - 1 and t % 2:
                        z_rest(i)
                    if 1 <= i <= PARTS - AHEAD:
                        weights_rest(i - 1 + AHEAD)
                if t % 2 == 0:
                    continue
                u = t // 2
                if u == 0:
                    dve.wait_ge(w_in, 16 * 4)
                    dve.wait_ge(w2_hi_ready, 1)
                    nc.vector.tensor_tensor(w2_lo[:], w2[:], w2_hi[:].bitcast(fp32), ALU.subtract
                                            ).then_inc(w2_lo_ready, 1)
                for n in range(H1 // P):
                    dve.wait_ge(h1_done, 4 * u + n + 1)
                    dve.wait_ge(h1_hi_ready, 4 * u + n + 1)
                    nc.vector.tensor_scalar(h1[:, n, :], bank[:, l1_bank[n], 0:PAIR], b1[:, n:n + 1], 0.0,
                                            ALU.add, ALU.max).then_inc(h1_ready, 1)
                    dve.wait_ge(h1_ready, 4 * u + n + 1)
                    nc.vector.tensor_tensor(h1_lo[:, n, :], h1[:, n, :], h1_hi[:, n, :].bitcast(fp32), ALU.subtract
                                            ).then_inc(h1_lo_ready, 1)
                    if t < NT - 1:
                        keep_groups(t + 1, AFTER_LAYER1[n])
                dve.wait_ge(h2_done, 2 * u + 2)
                nc.vector.tensor_scalar(h2[:, 1, :], bank[:, 3, 0:PAIR], b2[:, 1:2], 0.0, ALU.add, ALU.max
                                        ).then_inc(h2_dve, 1)

        @block.scalar
        def _(act):
            def keep_groups(t, qs):
                for q in qs:
                    n = t * len(GROUPS) + q
                    if n % 2 == 0:
                        act.wait_ge(transposed, n + 1)
                        nc.scalar.copy(group_places(t, q), group_bank(t, q)).then_inc(kept_act, 1)

            def keep_table(k):
                act.wait_ge(one_hot_used, C * (k + 1))
                nc.scalar.copy(e_t[:, :, 1 + k], bank[:, 6 + k % 2, :]).then_inc(table_kept, 1)

            def round_table(k, h):
                cols = half_cols(h)
                act.wait_ge(table_in[k % TABLE_RING][h], 32 * (k // TABLE_RING + 1))
                if k >= SPLIT_RING:
                    act.wait_ge(one_hot_used, C * (k - SPLIT_RING + 1))
                nc.scalar.copy(table_hi[0:KR, k % SPLIT_RING, cols], table[0:KR, k % TABLE_RING, cols]
                               ).then_inc(hi_ready, 1)

            def make_one_hot(k, c, half):
                made = made_by_act(k, c)
                if c == ACT_CHUNKS[k][0]:
                    act.wait_ge(ids_in[k % TABLE_RING], 16 * (k // TABLE_RING + 1))
                if made:
                    act.wait_ge(one_hot_act, made)
                nc.scalar.activation(square[0:KR, :], ids_all[0:KR, k % TABLE_RING, :], ACT.Square,
                                     bias=minus_row_no[0:KR, c:c + 1]).then_inc(squared, 1)
                for h in half:
                    if k + 1 < len(ONE_HOT):
                        round_table(k + 1, h)
                    else:
                        keep_groups(0, [2 * h])
                n = C * k + c
                if n >= OH_RING:
                    act.wait_ge(one_hot_used, n - OH_RING + 1)
                act.wait_ge(squared, made + 1)
                nc.scalar.activation(one_hot[0:KR, n % OH_RING, :], square[0:KR, :], ACT.Relu,
                                     bias=one[0:KR, :], scale=-2.0).then_inc(one_hot_act, 1)

            round_table(0, 0)
            round_table(0, 1)
            act.wait_ge(row_no_ready, 3)
            for k in range(len(ONE_HOT)):
                halves = [[0, 1]] if len(ACT_CHUNKS[k]) == 1 else [[0], [1]]
                for c, half in zip(ACT_CHUNKS[k], halves):
                    make_one_hot(k, c, half)
                if k >= 1:
                    keep_table(k - 1)
                if k == 2:
                    act.wait_ge(dense_in, 16)
                    nc.scalar.copy(e_t[:, :, 0], dense[:]).then_inc(dense_ready, 1)
                    nc.scalar.copy(e_t[:, :, F], dense[:]).then_inc(copies_ready, 1)
                if k == 4:
                    nc.scalar.copy(dense_hi[:], dense[:]).then_inc(dense_hi_ready, 1)
                    act.wait_ge(table_kept, 1)
                    nc.scalar.copy(e_t[:, :, F + 1], e_t[:, :, 1]).then_inc(copies_ready, 1)

            def round_weights(i):
                if i == 0:
                    act.wait_ge(w1_early, 16)
                if i == len(EARLY):
                    act.wait_ge(w1_summed, 1)
                if i == 1 + len(EARLY):
                    act.wait_ge(w1_late, 16)
                c = W1_ORDER[i]
                nc.scalar.copy(w1_hi[:, c, :], w1[:, c, :]).then_inc(w1_hi_ready, 1)

            keep_groups(0, range(4, len(GROUPS)))
            round_weights(0)
            keep_table(len(ONE_HOT) - 1)
            keep_groups(1, [0, 1])
            for i in range(1, AHEAD):
                round_weights(i)
            for t in range(NT):
                for q in range(NQ):
                    i = NQ * t + q
                    if t == NT - 2 and q == NQ - 1:
                        keep_groups(t + 1, range(4, len(GROUPS)))
                    act.wait_ge(gram_done, i + 1)
                    if i >= NQ:
                        act.wait_ge(z_lo_ready, i - NQ + 1)
                    take_interactions(nc.scalar.copy, act, folded_act, t, q, (2, 3)).then_inc(z_act, 1)
                    act.wait_ge(z_act, i + 1)
                    nc.scalar.copy(z_quarter(z_hi, t, q, 2, 4), z_quarter(z, t, q, 2, 4)).then_inc(z_hi_act, 1)
                    if t < NT - 1:
                        keep_groups(t + 1, AFTER_QUARTER[t][q])
                    if i + AHEAD < PARTS:
                        round_weights(i + AHEAD)
                if t % 2 == 0:
                    continue
                u = t // 2
                if u == 0:
                    act.wait_ge(w_in, 16 * 4)
                    nc.scalar.copy(w2_hi[:], w2[:]).then_inc(w2_hi_ready, 1)
                for n in range(H1 // P):
                    act.wait_ge(h1_done, 4 * u + n + 1)
                    nc.scalar.activation(h1_hi[:, n, :], bank[:, l1_bank[n], 0:PAIR], ACT.Relu, bias=b1[:, n:n + 1]
                                         ).then_inc(h1_hi_ready, 1)
                    if t < NT - 1:
                        keep_groups(t + 1, AFTER_LAYER1[n])
                act.wait_ge(h2_done, 2 * u + 1)
                nc.scalar.activation(h2[:, 0, :], bank[:, 2, 0:PAIR], ACT.Relu, bias=b2[:, 0:1]).then_inc(h2_act, 1)
                act.wait_ge(y_done, u + 1)
                nc.scalar.copy(y[:, u * PAIR:(u + 1) * PAIR], bank[0:1, 2, PAIR:2 * PAIR]).then_inc(y_kept, 1)

        @block.tensor
        def _(pe):
            def transpose_groups(t, qs):
                for q in qs:
                    n = t * len(GROUPS) + q
                    pe.wait_ge(rows_in[t][q], 16 * len(GROUPS[q]))
                    if t == 1 and q in (1, 2):
                        pe.wait_ge(table_kept, len(ONE_HOT) - 2 + q)
                    elif n > len(GROUPS) + 2:
                        wait_groups(pe, n - 1)
                    for i in range(len(GROUPS[q])):
                        last = nc.tensor.transpose(group_bank(t, q)[:, i, :], rows[:, t % 2, 4 * q + i, :], ident[:])
                    last.then_inc(transposed, 1)

            pe.wait_ge(ident_ready, 1)
            n = 0
            for k in range(len(ONE_HOT)):
                q = k - len(ONE_HOT) + len(GROUPS)
                if q >= 0:
                    transpose_groups(0, [q])
                if k >= 2:
                    pe.wait_ge(table_kept, k - 1)
                for c in range(C):
                    if c in (0, C // 2):
                        pe.wait_ge(hi_ready, 2 * k + int(c > 0) + 1)
                    if c in ACT_CHUNKS[k]:
                        pe.wait_ge(one_hot_act, made_by_act(k, c) + 1)
                    else:
                        pe.wait_ge(one_hot_dve, made_by_dve(k, c) + 1)
                    rows_c = slice(c * D, (c + 1) * D)
                    nc.tensor.matmul(bank[:, 6 + k % 2, :], table_hi[0:KR, k % SPLIT_RING, rows_c],
                                     one_hot[0:KR, n % OH_RING, :], start=c == 0, stop=False)
                    if c in (0, C // 2):
                        pe.wait_ge(lo_ready, 2 * k + int(c > 0) + 1)
                    nc.tensor.matmul(bank[:, 6 + k % 2, :], table_lo[0:KR, k % SPLIT_RING, rows_c],
                                     one_hot[0:KR, n % OH_RING, :], start=False, stop=c == C - 1
                                     ).then_inc(one_hot_used, 1)
                    n += 1
            transpose_groups(1, [0, 1])
            for t in range(NT):
                u = t // 2
                wait_groups(pe, (t + 1) * len(GROUPS))
                if t == 0:
                    pe.wait_ge(pad_ready, 1)
                    pe.wait_ge(dense_ready, 1)
                    pe.wait_ge(copies_ready, FOLDED)
                    pe.wait_ge(table_kept, len(ONE_HOT))
                for q in range(NQ):
                    i = t % 2 * NQ + q
                    if (t, q) == (0, 2):
                        wait_groups(pe, len(GROUPS) + 1)
                    if i >= 3:
                        pe.wait_ge(z_act, NQ * t + q - 2)
                        pe.wait_ge(z_dve, NQ * t + q - 2)
                    elif i == 1 and u:
                        pe.wait_ge(y_kept, u)
                    for g in range(QS // 4):
                        if t == NT - 2 and q == NQ - 1 and g == QS // 4 - 3:
                            transpose_groups(t + 1, range(4, len(GROUPS)))
                        b0 = t * P + q * QS + 4 * g
                        last = nc.tensor.matmul(gram[:, i % 3, g, 0:4 * F],
                                                e_t[:, b0:b0 + 4, :].rearrange("p s f -> p (s f)"),
                                                e_t[:, b0:b0 + 4, 0:F], start=True, stop=True)
                    last.then_inc(gram_done, 1)
                    if t < NT - 1:
                        transpose_groups(t + 1, AFTER_QUARTER[t][q])
                if t % 2 == 0:
                    continue
                cols = slice(u * PAIR, (u + 1) * PAIR)

                def layer1(n, weights, part, x, start=False, stop=False):
                    return nc.tensor.matmul(bank[:, l1_bank[n], 0:PAIR], weights[:, part, n * P:(n + 1) * P], x,
                                            start=start, stop=stop)

                if u == 0:
                    pe.wait_ge(dense_lo_ready, 1)
                    pe.wait_ge(w1_hi_ready, PARTS)
                    pe.wait_ge(w1_lo_ready, PARTS)
                for n in range(H1 // P):
                    if n % 2 == 0:
                        pe.wait_ge(z_act, NQ * t + 2 + n // 2)
                        pe.wait_ge(z_dve, NQ * t + 2 + n // 2)
                    layer1(n, w1_hi, SLOTS, dense_hi[:, cols], start=True)
                    layer1(n, w1_hi, SLOTS, dense_lo[:, cols])
                    layer1(n, w1_lo, SLOTS, dense_hi[:, cols])
                pe.wait_ge(z_hi_act, NQ * (t + 1))
                pe.wait_ge(z_hi_dve, NQ * (t + 1))
                for n in range(H1 // P):
                    for c in range(SLOTS):
                        layer1(n, w1_hi, c, z_hi[:, c, :])
                        layer1(n, w1_lo, c, z_hi[:, c, :])
                    if n == 0:
                        pe.wait_ge(z_lo_ready, NQ * (t + 1))
                    for c in range(SLOTS):
                        last = layer1(n, w1_hi, c, z_lo[:, c, :], stop=c == SLOTS - 1)
                    last.then_inc(h1_done, 1)
                    if t < NT - 1:
                        transpose_groups(t + 1, AFTER_LAYER1[n])
                if u == 0:
                    pe.wait_ge(w2_hi_ready, 1)
                    pe.wait_ge(w2_lo_ready, 1)
                for n, m in LAYER2_ORDER:
                    pe.wait_ge(h1_hi_ready, 4 * u + n + 1)
                    pe.wait_ge(h1_lo_ready, 4 * u + n + 1)
                    h2_sum = bank[:, 2 + m, 0:PAIR]
                    m_cols = slice(m * P, (m + 1) * P)
                    nc.tensor.matmul(h2_sum, w2_hi[:, n, m_cols], h1_hi[:, n, :], start=n == 0, stop=False)
                    nc.tensor.matmul(h2_sum, w2_lo[:, n, m_cols], h1_hi[:, n, :], start=False, stop=False)
                    last = nc.tensor.matmul(h2_sum, w2_hi[:, n, m_cols], h1_lo[:, n, :], start=False,
                                            stop=n == H1 // P - 1)
                    if n == H1 // P - 1:
                        last.then_inc(h2_done, 1)
                y_row = bank[0:1, 2, PAIR:2 * PAIR]
                pe.wait_ge(h2_act, u + 1)
                nc.tensor.matmul(y_row, w3[:, 0:1], h2[:, 0, :], start=True, stop=False)
                pe.wait_ge(h2_dve, u + 1)
                nc.tensor.matmul(y_row, w3[:, 1:2], h2[:, 1, :], start=False, stop=True).then_inc(y_done, 1)


def kernel(**inputs):
    import numpy as np
    import concourse.bacc as bacc
    from concourse.bass_utils import run_bass_kernel_spmd

    ids = np.asarray(inputs["ids"])
    w1 = np.asarray(inputs["W_top1"])
    pairs = D + F * (F - 1) // 2
    w1_laid = np.zeros((P, SLOTS, H1), w1.dtype)
    for p, c, row in pair_rows():
        w1_laid[p, c] = w1[row]
    laid_out = {
        "dense_t": np.asarray(inputs["r_dense_features"]).T,
        "idx": ids.reshape(NT, P, NUM_SPARSE).transpose(1, 0, 2),
        "oh_ids": ids.T[ONE_HOT],
        "w1": w1_laid,
        "wd": np.stack([w1[0:D], w1[pairs:pairs + D]]),
        "b1": np.asarray(inputs["b_top1"]).reshape(H1 // P, P).T,
        "w2": np.asarray(inputs["W_top2"]).reshape(H1 // P, P, H2).transpose(1, 0, 2),
        "b2": np.asarray(inputs["b_top2"]).reshape(H2 // P, P).T,
        "w3": np.asarray(inputs["W_top3"]).reshape(H2 // P, P).T,
    }
    laid_out.update({f"tbl_{i}": inputs[f"tbl_{i}"] for i in range(NUM_SPARSE)})

    nc = bacc.Bacc("TRN2", target_bir_lowering=False, num_devices=1)
    arrays, dram = {}, {}
    for name, a in laid_out.items():
        a = np.ascontiguousarray(a)
        arrays[f"in_{name}"] = a
        dram[name] = nc.dram_tensor(f"in_{name}", a.shape, mybir.dt.from_np(a.dtype), kind="ExternalInput").ap()
    out = nc.dram_tensor("out_y", (1, BATCH), mybir.dt.float32, kind="ExternalOutput").ap()
    dlrm_tower(nc, dram["dense_t"], dram["idx"], dram["oh_ids"], [dram[f"tbl_{i}"] for i in range(NUM_SPARSE)],
               dram["w1"], dram["wd"], dram["b1"], dram["w2"], dram["b2"], dram["w3"], out)
    result = run_bass_kernel_spmd(nc, [arrays], core_ids=[0])
    return result.results[0]["out_y"].reshape(BATCH, 1)
```
